# Optimizing a Trainium2 kernel written in Bass

```python
import numpy as np
import jax
import jax.numpy as jnp

def _softmax(x, axis=-1):
    return jax.nn.softmax(x, axis=axis)
def _gelu(x):
    return jax.nn.gelu(x, approximate=True)
def _silu(x):
    return jax.nn.silu(x)
def _sigmoid(x):
    return jax.nn.sigmoid(x)
def _layernorm(x, axis=-1, eps=1e-5):
    m = jnp.mean(x, axis=axis, keepdims=True)
    v = jnp.var(x, axis=axis, keepdims=True)
    return (x - m) / jnp.sqrt(v + eps)
def _scatter_add(tgt, idx, src, axis=0):
    return tgt.at[idx].add(src)
def _segment_sum(src, seg, n):
    return jax.ops.segment_sum(src, seg, n)

kernel_name = 'mk_adj_preln_d2_adj_256_6af9d3'

def setup_inputs(seed: int = 0):
    np.random.seed(seed)
    _w = jnp.asarray
    def _rec_inputs():
        import jax
        import jax.numpy as jnp
        _gk = jax.random.key(seed)
        x = -0.0002928 + 1 * jax.random.normal(jax.random.fold_in(_gk, 1), (128, 128, 256), jnp.float32)
        _a = jax.random.bernoulli(jax.random.fold_in(_gk, 2), 0.03125, (128, 128, 128))
        _a = jnp.logical_or(_a, jnp.swapaxes(_a, -1, -2))
        _a = jnp.logical_or(_a, jnp.eye(128, dtype=bool))
        _af = _a.astype(jnp.float32)
        _af = _af * jax.random.uniform(jax.random.fold_in(_gk, 3), (128, 128, 128), jnp.float32, 0.05, 1)
        adj = _af
        return x, adj
    x, adj = _rec_inputs()
    def _L0_gnn_setup():
        import jax, jax.numpy as jnp
        import numpy as np
        key = jax.random.key(seed)
        k1, k2, k3, k4 = jax.random.split(key, 4)
        B, N, F_in, F_out = (8, 2048, 256, 256)
        x = jax.random.normal(k1, (B, N, F_in), dtype=jnp.float32)
        adj = jax.random.uniform(k2, (B, N, N), dtype=jnp.float32)
        stdv = 1.0 / np.sqrt(F_out)
        weight = jax.random.uniform(k3, (F_in, F_out), dtype=jnp.float32, minval=-stdv, maxval=stdv)
        bias = jax.random.uniform(k4, (F_out,), dtype=jnp.float32, minval=-stdv, maxval=stdv)
        return {'x': x, 'adj': adj, 'weight': weight, 'bias': bias}
    _L0_gnn_all = _L0_gnn_setup()
    _L0_gnn_in = {k: v for k, v in _L0_gnn_all.items() if k in ('weight', 'bias', )}
    del _L0_gnn_all

    def _L1_gnn_setup():
        import jax, jax.numpy as jnp
        import numpy as np
        DIM = 256
        HEADS = 8
        BS = 8
        N = 1024
        NEG = -1000000000.0
        key = jax.random.key(seed)
        ks = jax.random.split(key, 8)
        feats = jax.random.normal(ks[0], (BS, N, DIM), dtype=jnp.float32)
        adj_mat = (jax.random.uniform(ks[1], (BS, N, N)) < 0.1).astype(jnp.float32)
        s = 1.0 / np.sqrt(DIM)
        fc_w = jax.random.normal(ks[2], (DIM, DIM * HEADS), dtype=jnp.float32) * s
        fc_b = jnp.zeros((DIM * HEADS,), dtype=jnp.float32)
        q_w = jax.random.normal(ks[3], (DIM, 1), dtype=jnp.float32) * s
        q_b = jnp.zeros((1,), dtype=jnp.float32)
        k_w = jax.random.normal(ks[4], (DIM, 1), dtype=jnp.float32) * s
        k_b = jnp.zeros((1,), dtype=jnp.float32)
        fp_w = jax.random.normal(ks[5], (DIM * HEADS, DIM), dtype=jnp.float32) * (1.0 / np.sqrt(DIM * HEADS))
        fp_b = jnp.zeros((DIM,), dtype=jnp.float32)
        return {'feats': feats, 'adj_mat': adj_mat, 'fc_w': fc_w, 'fc_b': fc_b, 'q_w': q_w, 'q_b': q_b, 'k_w': k_w, 'k_b': k_b, 'fp_w': fp_w, 'fp_b': fp_b}
    _L1_gnn_all = _L1_gnn_setup()
    _L1_gnn_in = {k: v for k, v in _L1_gnn_all.items() if k in ('fc_w', 'fc_b', 'q_w', 'q_b', 'k_w', 'k_b', 'fp_w', 'fp_b', )}
    del _L1_gnn_all

    return {
        "x": x,
        "adj": adj,
        "L0_gnn_weight": _L0_gnn_in["weight"],
        "L0_gnn_bias": _L0_gnn_in["bias"],
        "L1_gnn_fc_w": _L1_gnn_in["fc_w"],
        "L1_gnn_fc_b": _L1_gnn_in["fc_b"],
        "L1_gnn_q_w": _L1_gnn_in["q_w"],
        "L1_gnn_q_b": _L1_gnn_in["q_b"],
        "L1_gnn_k_w": _L1_gnn_in["k_w"],
        "L1_gnn_k_b": _L1_gnn_in["k_b"],
        "L1_gnn_fp_w": _L1_gnn_in["fp_w"],
        "L1_gnn_fp_b": _L1_gnn_in["fp_b"],
    }

def reference(x, adj, L0_gnn_weight, L0_gnn_bias, L1_gnn_fc_w, L1_gnn_fc_b, L1_gnn_q_w, L1_gnn_q_b, L1_gnn_k_w, L1_gnn_k_b, L1_gnn_fp_w, L1_gnn_fp_b):
    import jax
    import jax.numpy as jnp
    def _L0_gnn_ref(x, adj, weight, bias):
        import jax, jax.numpy as jnp
        import numpy as np
        support = jnp.einsum('bni,io->bno', x, weight)
        out = jnp.einsum('bnm,bmo->bno', adj, support)
        return out + bias

    def _L1_gnn_ref(feats, adj_mat, fc_w, fc_b, q_w, q_b, k_w, k_b, fp_w, fp_b):
        import jax, jax.numpy as jnp
        import numpy as np
        DIM = 256
        HEADS = 8
        BS = 8
        N = 1024
        NEG = -1000000000.0
        bs, n, dim = feats.shape
        feat_proj = (feats @ fc_w + fc_b).reshape(bs, n, HEADS, dim).transpose(0, 2, 1, 3)
        q = feat_proj @ q_w + q_b
        k = feat_proj @ k_w + k_b
        logits = q + jnp.swapaxes(k, -1, -2)
        masked = logits + (1.0 - adj_mat[:, None]) * NEG
        masked = jax.nn.leaky_relu(masked, negative_slope=0.01)
        attn = jax.nn.softmax(masked, axis=-1)
        out = attn @ feat_proj
        out = out.transpose(0, 2, 1, 3).reshape(bs, n, HEADS * dim)
        out = out @ fp_w + fp_b + feats
        return jax.nn.sigmoid(out)

    h = jnp.maximum(_layernorm(x, axis=-1), 0.0)
    x = x + _L0_gnn_ref(h, adj, L0_gnn_weight, L0_gnn_bias)
    h = jnp.maximum(_layernorm(x, axis=-1), 0.0)
    x = x + _L1_gnn_ref(h, adj, L1_gnn_fc_w, L1_gnn_fc_b, L1_gnn_q_w, L1_gnn_q_b, L1_gnn_k_w, L1_gnn_k_b, L1_gnn_fp_w, L1_gnn_fp_b)
    return x


_drawn_inputs = setup_inputs


def setup_inputs(seed=0):
    import zlib

    import numpy as np

    out = dict(_drawn_inputs(seed))
    spreads = {'L1_gnn_fc_b': (0.0, 0.661), 'L1_gnn_fp_b': (0.0, 0.646)}
    factors = {'L0_gnn_bias': 2.747}
    for name, (base, spread) in spreads.items():
        noise = np.random.default_rng([zlib.crc32(name.encode()), seed]).standard_normal(out[name].shape)
        drawn = base * np.exp(spread * noise) if base else spread * noise
        out[name] = jnp.asarray(drawn.astype(out[name].dtype))
    for name, factor in factors.items():
        out[name] = (out[name] * factor).astype(out[name].dtype)
    return out
```

```python
from contextlib import ExitStack

import concourse.bass as bass
from concourse import mybir

F32 = mybir.dt.float32
F32R = mybir.dt.float32r
ALU = mybir.AluOpType
ACT = mybir.ActivationFunctionType
AX = mybir.AxisListType

P = 128
D = 256
DT = D // P
H = 8
J = 2
NEG = 1.0e9
SLOPE = 0.01
EPS = 1e-5
BANK = 512
GC = H * D // BANK
HC = BANK // P
KQ = 32


def gnn_pair(nc, graph, identity, head_mask, row_coef, w0, bias0, fc_wT, fc_b, qk_w, q_b, k_b, fp_w, fp_b, out):
    NP = graph.shape[0]
    assert NP % 2 == 0 and NP >= 8

    def has(p):
        return not isinstance(p, int) or 0 <= p < NP

    with ExitStack() as ctx:
        def sb(name, shape, dt=F32):
            return ctx.enter_context(nc.sbuf_tensor(name, shape, dt))

        def psum(name, shape):
            return ctx.enter_context(nc.psum_tensor(name, shape, F32))

        def sem(name):
            return ctx.enter_context(nc.semaphore(name))

        def two(name, shape, dt=F32):
            return [sb(f"{name}{k}", shape, dt) for k in range(2)]

        ident = sb("ident", [P, P])
        hmask = sb("hmask", [P, H, P])
        coef = sb("coef", [P, 10])
        w0_f = sb("w0_f", [P, DT, D])
        w0_hi, w0_lo = sb("w0_hi", [P, DT, D], F32R), sb("w0_lo", [P, DT, D], F32R)
        b0_row = sb("b0_row", [P, D])
        m_hi, m_lo = sb("m_hi", [P, DT, H * D], F32R), sb("m_lo", [P, DT, H * D], F32R)
        u_f = sb("u_f", [P, J, DT, P])
        u_hi, u_lo = sb("u_hi", [P, J, DT, P], F32R), sb("u_lo", [P, J, DT, P], F32R)
        u_th = sb("u_th", [P, DT, 2, H])
        qk = sb("qk", [P, DT, 2])
        fcb = sb("fcb", [P, H * DT])
        kqb2 = sb("kqb2", [P, 2])
        kq_bias = sb("kq_bias", [P, 1])
        kq_tmp = sb("kq_tmp", [P, 2])
        c_row = sb("c_row", [P, D])
        neg_half, half, eps = sb("neg_half", [P, 1]), sb("half", [P, 1]), sb("eps", [P, 1])
        gate = sb("gate", [P, 6])

        g_in = two("g_in", [P, J * (D + 2 * P)])
        z0 = two("z0", [P, J, D])
        h0_hi, h0_lo = two("h0_hi", [P, J, D], F32R), two("h0_lo", [P, J, D], F32R)
        aT_hi, aT_lo = two("aT_hi", [P, J, P], F32R), two("aT_lo", [P, J, P], F32R)
        xb = two("xb", [P, J, D])
        t_neg = two("t_neg", [P, J, P])
        ah_hi, ah_lo = two("ah_hi", [P, J, DT, P], F32R), two("ah_lo", [P, J, DT, P], F32R)
        x1 = two("x1", [P, J, D])
        z1 = two("z1", [P, J, D])
        hT_hi, hT_lo = two("hT_hi", [P, J, DT, P], F32R), two("hT_lo", [P, J, DT, P], F32R)
        feats_c = two("feats_c", [P, J, D])
        x1_half = two("x1_half", [P, J, D])
        st0, mv0, rs0 = two("st0", [P, J, 6]), two("mv0", [P, J, 2]), two("rs0", [P, J])
        st1, mv1, rs1 = two("st1", [P, J, 6]), two("mv1", [P, J, 2]), two("rs1", [P, J])
        ve0, ve1 = two("ve0", [P, J]), two("ve1", [P, J])
        res = two("res", [P, J, D])

        kq_f, kq_h = sb("kq_f", [P, P]), sb("kq_h", [P, P], F32R)
        kq_t = sb("kq_t", [P, P], F32R)
        kq_k = sb("kq_k", [P, P])
        lq = two("lq", [P, P], F32R)
        rk = sb("rk", [P, H, P], F32R)
        att = two("att", [P, H, P])
        mx, lm, nlm = two("mx", [P, H]), two("lm", [P, H]), two("nlm", [P, H])
        esum, rinv = two("esum", [P, H]), two("rinv", [P, H])
        pT = two("pT", [P, H, P])
        gf = two("gf", [P, H * D])
        y, th = two("y", [P, D]), two("th", [P, D])

        fcT_sb = gf
        fp_sb = sb("fp_sb", [P, H * DT, D])
        fcb_wide = att
        fcb_rows = pT

        front = psum("front", [P, BANK])
        gbank = [psum(f"gbank{k}", [P, BANK]) for k in range(2)]
        sbank = [psum(f"sbank{j}", [P, H * P]) for j in range(J)]
        ybank = psum("ybank", [P, BANK])
        front_jt = front[:].rearrange("p (j t n) -> p j t n", j=J, t=DT)
        front_jd = front[:].rearrange("p (j d) -> p j d", j=J)

        s_const = sem("s_const")
        s_loaded = [sem("s_loaded0"), sem("s_loaded1")]
        s_stored = [sem("s_stored0"), sem("s_stored1")]
        v_set, a_set, pe_set, g_set = sem("v_set"), sem("a_set"), sem("pe_set"), sem("g_set")
        v_st0, v_mv0 = sem("v_st0"), sem("v_mv0")
        g_ve0, g_rs0, v_z0 = sem("g_ve0"), sem("g_rs0"), sem("v_z0")
        g_xb, v_t = sem("g_xb"), sem("v_t")
        a_h0hi, a_aThi = sem("a_h0hi"), sem("a_aThi")
        v_h0lo, g_aTlo = sem("v_h0lo"), sem("g_aTlo")
        pe_ah, a_ahhi, v_ahlo = sem("pe_ah"), sem("a_ahhi"), sem("v_ahlo")
        pe_out0, v_x1 = sem("pe_out0"), sem("v_x1")
        v_st1, v_mv1 = sem("v_st1"), sem("v_mv1")
        g_ve1, g_rs1, v_z1 = sem("g_ve1"), sem("g_rs1"), sem("v_z1")
        a_relu, g_feats, g_half = sem("a_relu"), sem("g_feats"), sem("g_half")
        pe_zT, a_hThi, v_hTlo = sem("pe_zT"), sem("a_hThi"), sem("v_hTlo")
        pe_kq, v_kqf, v_kqh, v_kqt = sem("pe_kq"), sem("v_kqf"), sem("v_kqh"), sem("v_kqt")
        v_kqk, v_rk, a_lq = sem("v_kqk"), sem("v_rk"), sem("a_lq")
        pe_s, v_mx, v_leaky = sem("pe_s"), sem("v_mx"), sem("v_leaky")
        v_lm, v_nlm = sem("v_lm"), sem("v_nlm")
        a_exp, v_rinv, g_norm = sem("a_exp"), sem("v_rinv"), sem("g_norm")
        pe_pT, a_pT = sem("pe_pT"), sem("a_pT")
        pe_g, a_g = sem("pe_g"), sem("a_g")
        pe_y, v_y, a_th, v_res = sem("pe_y"), sem("v_y"), sem("a_th"), sem("v_res")
        CONST = 13 * 16
        SETUP_V = H * DT + 7
        SETUP_A = H * DT + 2

        block = ctx.enter_context(nc.Block())

        def x_of(q):
            return g_in[q][:, 0:J * D].rearrange("p (j d) -> p j d", j=J)

        def adj_of(q):
            return g_in[q][:, J * D:J * D + J * P].rearrange("p (j n) -> p j n", j=J)

        def adjT_of(q):
            return g_in[q][:, J * D + J * P:].rearrange("p (j n) -> p j n", j=J)

        def pipeline(eng, step):
            for i in range(-2, 2):
                step(i, i % 2)
            with eng.Fori(2, NP - 4, 2) as i:
                step(i, 0)
                step(i + 1, 1)
            for i in range(NP - 4, NP + 1):
                step(i, i % 2)

        @block.sync
        def _(sp):
            for dst, src in ((fcT_sb[0][:].rearrange("p (t d) -> p t d", t=H), fc_wT[:, 0:H, :]),
                             (fcT_sb[1][:].rearrange("p (t d) -> p t d", t=H), fc_wT[:, H:2 * H, :]),
                             (fp_sb[:], fp_w), (qk[:], qk_w), (fcb[:], fc_b), (w0_f[:], w0), (ident[:], identity),
                             (coef[:], row_coef), (hmask[:], head_mask),
                             (b0_row[:], bias0.partition_broadcast(P)),
                             (c_row[:], fp_b.partition_broadcast(P)),
                             (kqb2[:, 0:1], k_b.partition_broadcast(P)),
                             (kqb2[:, 1:2], q_b.partition_broadcast(P))):
                sp.dma_start(dst, src).then_inc(s_const, 16)

            def step(i, q):
                p = i + 3
                if has(p):
                    if has(p - 2):
                        sp.wait_ge(v_st0, 2 * (p - 1))
                        sp.wait_ge(v_z0, 2 * (p - 1))
                        sp.wait_ge(g_xb, p - 1)
                        sp.wait_ge(v_t, p - 1)
                        sp.wait_ge(a_aThi, p - 1)
                        sp.wait_ge(g_aTlo, p - 1)
                    sp.dma_start(g_in[1 - q][:], graph[p]).then_inc(s_loaded[1 - q], 16)
                p = i - 1
                if has(p):
                    sp.wait_ge(v_res, 2 * (p + 1))
                    sp.dma_start(out[p], res[1 - q][:]).then_inc(s_stored[1 - q], 16)

            sp.dma_start(g_in[0][:], graph[0]).then_inc(s_loaded[0], 16)
            pipeline(sp, step)
            for q in range(2):
                sp.wait_ge(s_stored[q], 16 * (NP // 2))

        @block.tensor
        def _(pe):
            def split(out_ap, pairs, first=True, last=True):
                terms = [(w, m) for (wh, wl), (mh, ml) in pairs for w, m in ((wl, mh), (wh, ml), (wh, mh))]
                for n, (w, m) in enumerate(terms):
                    mm = pe.matmul(out_ap, w, m, start=first and n == 0, stop=last and n == len(terms) - 1)
                return mm

            def setup():
                pe.wait_ge(s_const, CONST)
                n = 0
                for h in range(H):
                    for dt in range(DT):
                        if n >= 2:
                            pe.wait_ge(v_set, n - 1)
                        bank = gbank[n % 2]
                        for cols, rhs in ((slice(0, D), None), (slice(D, D + 2), qk)):
                            for kt in range(DT):
                                t = h * DT + kt
                                w = fcT_sb[t // H][:].rearrange("p (t d) -> p t d", t=H)[:, t % H, dt * P:(dt + 1) * P]
                                m = fp_sb[:, t, :] if rhs is None else rhs[:, kt, :]
                                mm = pe.matmul(bank[:, cols], w, m, start=kt == 0, stop=kt == DT - 1)
                        mm.then_inc(pe_set, 1)
                        n += 1
                pe.wait_ge(g_set, 4)
                for t in range(H * DT):
                    pe.matmul(front[:, 0:D], fcb_wide[t // H][:, t % H, :], fp_sb[:, t, :],
                              start=t == 0, stop=t == H * DT - 1)
                for t in range(H * DT):
                    mm = pe.matmul(ybank[:, 0:2], fcb_rows[t // H][:, t % H, :], qk[:, t % DT, :],
                                   start=t == 0, stop=t == H * DT - 1)
                mm.then_inc(pe_set, 1)
                pe.wait_ge(v_set, SETUP_V)
                pe.wait_ge(a_set, SETUP_A)

            def aggregate(p, q):
                pe.wait_ge(v_h0lo, p + 1)
                pe.wait_ge(a_aThi, p + 1)
                pe.wait_ge(g_aTlo, p + 1)
                if has(p - 1):
                    pe.wait_ge(v_kqf, p)
                for j in range(J):
                    for dt in range(DT):
                        s = slice(dt * P, (dt + 1) * P)
                        mm = split(front_jt[:, j, dt, :],
                                   [((h0_hi[q][:, j, s], h0_lo[q][:, j, s]), (aT_hi[q][:, j, :], aT_lo[q][:, j, :]))])
                mm.then_inc(pe_ah, 1)

            def transform(p, q):
                pe.wait_ge(v_ahlo, p + 1)
                for j in range(J):
                    mm = split(front_jd[:, j, :],
                               [((ah_hi[q][:, j, dt, :], ah_lo[q][:, j, dt, :]), (w0_hi[:, dt, :], w0_lo[:, dt, :]))
                                for dt in range(DT)])
                mm.then_inc(pe_out0, 1)

            def transpose_z(p, q):
                pe.wait_ge(v_z1, 2 * (p + 1))
                for j in range(J):
                    for dt in range(DT):
                        mm = pe.transpose(front_jt[:, j, dt, :], z1[q][:, j, dt * P:(dt + 1) * P], ident[:])
                mm.then_inc(pe_zT, 1)

            def queries_keys(p, q):
                pe.wait_ge(v_hTlo, p + 1)
                mm = split(front[:, 0:P],
                           [((u_hi[:, j, dt, :], u_lo[:, j, dt, :]), (hT_hi[q][:, j, dt, :], hT_lo[q][:, j, dt, :]))
                            for j in range(J) for dt in range(DT)])
                mm.then_inc(pe_kq, 1)

            def scores(p, j):
                if j == 0:
                    pe.wait_ge(v_rk, p + 1)
                    pe.wait_ge(a_lq, 2 * (p + 1))
                if has(p - 1):
                    pe.wait_ge(a_pT, 4 * (p - 1) + 2 * j + 2)
                for c in range(H // HC):
                    mm = pe.matmul(sbank[j][:, c * BANK:(c + 1) * BANK], lq[j][:], rk[:, c * HC:(c + 1) * HC, :],
                                   start=True, stop=True)
                mm.then_inc(pe_s, 1)

            def project(p, q, j, c):
                n = GC * j + c
                if n >= 2:
                    pe.wait_ge(a_g, 2 * GC * p + n - 1)
                elif has(p - 1):
                    pe.wait_ge(a_g, 2 * GC * p + n - 1)
                s = slice(c * BANK, (c + 1) * BANK)
                split(gbank[n % 2][:],
                      [((hT_hi[q][:, j, dt, :], hT_lo[q][:, j, dt, :]), (m_hi[:, dt, s], m_lo[:, dt, s]))
                       for dt in range(DT)]).then_inc(pe_g, 1)

            def transpose_p(p, j):
                pe.wait_ge(g_norm, 2 * p + j + 1)
                for h in range(H):
                    mm = pe.transpose(sbank[j][:, h * P:(h + 1) * P], att[j][:, h, :], ident[:])
                mm.then_inc(pe_pT, 1)

            def attend(p, j):
                pe.wait_ge(a_pT, 4 * p + 2 * j + 2)
                pe.wait_ge(a_g, 2 * GC * p + GC * (j + 1))
                if j or has(p - 1):
                    pe.wait_ge(v_y, 2 * p + j)
                for h in range(H):
                    mm = pe.matmul(ybank[:, 0:D], pT[j][:, h, :], gf[j][:, h * D:(h + 1) * D],
                                   start=h == 0, stop=h == H - 1)
                mm.then_inc(pe_y, 1)

            def step(i, q):
                if has(i + 1):
                    aggregate(i + 1, 1 - q)
                if has(i):
                    project(i, q, 0, 0)
                    project(i, q, 0, 1)
                    project(i, q, 0, 2)
                if has(i + 1):
                    transform(i + 1, 1 - q)
                if has(i):
                    project(i, q, 0, 3)
                    project(i, q, 1, 0)
                    project(i, q, 1, 1)
                if has(i + 1):
                    transpose_z(i + 1, 1 - q)
                if has(i):
                    project(i, q, 1, 2)
                    transpose_p(i, 0)
                if has(i + 1):
                    queries_keys(i + 1, 1 - q)
                if has(i):
                    attend(i, 0)
                    transpose_p(i, 1)
                    project(i, q, 1, 3)
                if has(i + 1):
                    scores(i + 1, 0)
                    scores(i + 1, 1)
                if has(i):
                    attend(i, 1)

            setup()
            pipeline(pe, step)

        @block.vector
        def _(dve):
            def setup():
                dve.wait_ge(s_const, CONST)
                n = 0
                for h in range(H):
                    for dt in range(DT):
                        dve.wait_ge(a_set, n + 1)
                        dve.tensor_copy(u_th[:, dt, :, h], gbank[n % 2][:, D:D + 2])
                        s = slice(h * D, (h + 1) * D)
                        dve.tensor_tensor(m_lo[:, dt, s], gbank[n % 2][:, 0:D], m_hi[:, dt, s].bitcast(F32),
                                          ALU.subtract).then_inc(v_set, 1)
                        n += 1
                dve.wait_ge(v_set, n)
                dve.wait_ge(g_set, 3)
                for j in range(J):
                    for dt in range(DT):
                        rows = u_f[:, j, dt, KQ * j:KQ * (j + 1)].rearrange("p (k c h) -> p k c h", k=2, c=2)
                        dve.tensor_copy(rows, u_th[:, dt, :, :].unsqueeze(2).broadcast_to([P, 2, 2, H]))\
                           .then_inc(v_set, 1)
                dve.wait_ge(a_set, n + 2)
                dve.tensor_tensor(u_lo[:], u_f[:], u_hi[:].bitcast(F32), ALU.subtract)
                dve.tensor_tensor(w0_lo[:], w0_f[:], w0_hi[:].bitcast(F32), ALU.subtract)
                dve.wait_ge(pe_set, n + 1)
                dve.tensor_tensor(kq_tmp[:], ybank[:, 0:2], kqb2[:], ALU.add).then_inc(v_set, 1)
                dve.wait_ge(v_set, n + 5)
                dve.tensor_tensor(kq_tmp[:], kq_tmp[:], coef[:, 0:2], ALU.mult).then_inc(v_set, 1)
                dve.wait_ge(v_set, n + 6)
                dve.tensor_tensor(kq_bias[:], kq_tmp[:, 0:1], kq_tmp[:, 1:2], ALU.add)
                dve.tensor_tensor(c_row[:], c_row[:], front[:, 0:D], ALU.add).then_inc(v_set, 1)

            def norm0(p, q):
                dve.wait_ge(s_loaded[q], 8 * (p - q) + 16)
                for j in range(J):
                    dve.bn_stats(st0[q][:, j, :], x_of(q)[:, j, :]).then_inc(v_st0, 1)
                dve.wait_ge(v_st0, 2 * (p + 1))
                if has(p - 2):
                    dve.wait_ge(v_z0, 2 * (p - 1))
                dve.memset(gate[:, q:q + 1], 0.0)
                for j in range(J):
                    dve.bn_aggr(mv0[q][:, j, :], st0[q][:, j, :]).then_inc(v_mv0, 1)

            def mask_term(p, q):
                if has(p - 2):
                    dve.wait_ge(v_mx, 2 * (p - 1))
                dve.tensor_scalar(t_neg[q][:], adj_of(q), 1.0, NEG, ALU.subtract, ALU.mult).then_inc(v_t, 1)

            def scale0(p, q):
                dve.wait_ge(g_rs0, p + 1)
                if has(p - 2):
                    dve.wait_ge(v_h0lo, p - 1)
                for j in range(J):
                    dve.tensor_scalar(z0[q][:, j, :], x_of(q)[:, j, :], mv0[q][:, j, 0:1], rs0[q][:, j:j + 1],
                                      ALU.subtract, ALU.mult).then_inc(v_z0, 1)

            def h0_low(p, q):
                dve.wait_ge(a_h0hi, p + 1)
                if has(p - 2):
                    dve.wait_ge(pe_ah, p - 1)
                dve.scalar_tensor_tensor(out=h0_lo[q][:], in0=z0[q][:], scalar=0.0, in1=h0_hi[q][:].bitcast(F32),
                                         op0=ALU.max, op1=ALU.subtract).then_inc(v_h0lo, 1)

            def ah_low(p, q):
                dve.wait_ge(a_ahhi, p + 1)
                if has(p - 2):
                    dve.wait_ge(pe_out0, p - 1)
                dve.tensor_tensor(ah_lo[q][:], front_jt[:], ah_hi[q][:].bitcast(F32), ALU.subtract)\
                   .then_inc(v_ahlo, 1)

            def residual0(p, q):
                dve.wait_ge(pe_out0, p + 1)
                dve.wait_ge(g_xb, p + 1)
                if has(p - 2):
                    dve.wait_ge(g_half, p - 1)
                dve.tensor_tensor(x1[q][:], front_jd[:], xb[q][:], ALU.add).then_inc(v_x1, 1)
                dve.wait_ge(v_x1, p + 1)
                for j in range(J):
                    dve.bn_stats(st1[q][:, j, :], x1[q][:, j, :]).then_inc(v_st1, 1)
                dve.wait_ge(v_st1, 2 * (p + 1))
                dve.memset(gate[:, 2 + q:3 + q], 0.0)
                for j in range(J):
                    dve.bn_aggr(mv1[q][:, j, :], st1[q][:, j, :]).then_inc(v_mv1, 1)

            def norm1(p, q):
                dve.wait_ge(g_rs1, p + 1)
                if has(p - 2):
                    dve.wait_ge(pe_zT, p - 1)
                    dve.wait_ge(a_relu, p - 1)
                for j in range(J):
                    dve.tensor_scalar(z1[q][:, j, :], x1[q][:, j, :], mv1[q][:, j, 0:1], rs1[q][:, j:j + 1],
                                      ALU.subtract, ALU.mult).then_inc(v_z1, 1)

            def hT_low(p, q):
                dve.wait_ge(a_hThi, p + 1)
                if has(p - 2):
                    dve.wait_ge(pe_g, 2 * GC * (p - 1))
                dve.scalar_tensor_tensor(out=hT_lo[q][:].rearrange("p j t n -> p (j t n)"), in0=front[:], scalar=0.0,
                                         in1=hT_hi[q][:].rearrange("p j t n -> p (j t n)").bitcast(F32),
                                         op0=ALU.max, op1=ALU.subtract).then_inc(v_hTlo, 1)

            def score_operands(p):
                dve.wait_ge(pe_kq, p + 1)
                dve.tensor_scalar(kq_f[:], front[:, 0:P], kq_bias[:, 0:1], None, ALU.add).then_inc(v_kqf, 1)
                dve.wait_ge(v_kqf, p + 1)
                dve.tensor_copy(kq_h[:], kq_f[:]).then_inc(v_kqh, 1)
                dve.wait_ge(v_kqh, p + 1)
                if has(p - 1):
                    dve.wait_ge(a_lq, 2 * p)
                dve.scalar_tensor_tensor(out=kq_t[:], in0=kq_h[:].bitcast(F32), scalar=coef[:, 2:3], in1=kq_f[:],
                                         op0=ALU.mult, op1=ALU.add).then_inc(v_kqt, 1)
                dve.wait_ge(v_kqt, p + 1)
                dve.tensor_scalar(kq_k[:], kq_t[:].bitcast(F32), coef[:, 3:4], coef[:, 4:5], ALU.mult, ALU.add)\
                   .then_inc(v_kqk, 1)
                dve.wait_ge(v_kqk, p + 1)
                if has(p - 1):
                    dve.wait_ge(pe_s, 2 * p)
                dve.tensor_tensor(rk[:], hmask[:], kq_k[:].unsqueeze(1).broadcast_to([P, H, P]), ALU.mult)\
                   .then_inc(v_rk, 1)

            def mask_max(p, q, j):
                dve.wait_ge(pe_s, 2 * p + j + 1)
                dve.wait_ge(v_t, p + 1)
                if has(p - 1):
                    dve.wait_ge(pe_pT, 2 * (p - 1) + j + 1)
                    dve.wait_ge(v_leaky, 2 * p)
                dve.memset(gate[:, 4 + j:5 + j], 0.0)
                for h in range(H):
                    r = dve.tensor_tensor_reduce(att[j][:, h, :], sbank[j][:, h * P:(h + 1) * P], t_neg[q][:, j, :],
                                                 1.0, -3.0e38, ALU.add, ALU.max, mx[j][:, h:h + 1])
                r.then_inc(v_mx, 1)

            def leaky(p, j):
                dve.wait_ge(v_mx, 2 * p + j + 1)
                dve.scalar_tensor_tensor(out=lm[j][:], in0=mx[j][:], scalar=SLOPE, in1=mx[j][:],
                                         op0=ALU.mult, op1=ALU.max).then_inc(v_lm, 1)
                dve.scalar_tensor_tensor(out=att[j][:], in0=att[j][:], scalar=SLOPE, in1=att[j][:],
                                         op0=ALU.mult, op1=ALU.max).then_inc(v_leaky, 1)
                dve.wait_ge(v_lm, 2 * p + j + 1)
                if has(p - 1):
                    dve.wait_ge(a_exp, 2 * (p - 1) + j + 1)
                dve.tensor_scalar(nlm[j][:], lm[j][:], -1.0, None, ALU.mult).then_inc(v_nlm, 1)

            def inverse(p, j):
                dve.wait_ge(a_exp, 2 * p + j + 1)
                if has(p - 1):
                    dve.wait_ge(g_norm, 2 * (p - 1) + j + 1)
                dve.reciprocal(rinv[j][:], esum[j][:]).then_inc(v_rinv, 1)

            def add_feats(p, q, j):
                dve.wait_ge(pe_y, 2 * p + j + 1)
                dve.wait_ge(g_feats, p + 1)
                if has(p - 1):
                    dve.wait_ge(a_th, 2 * (p - 1) + j + 1)
                dve.tensor_tensor(y[j][:], ybank[:, 0:D], feats_c[q][:, j, :], ALU.add).then_inc(v_y, 1)

            def residual1(p, q, j):
                dve.wait_ge(a_th, 2 * p + j + 1)
                dve.wait_ge(g_half, p + 1)
                if j == 0 and has(p - 2):
                    dve.wait_ge(s_stored[q], 8 * (p - q))
                dve.scalar_tensor_tensor(out=res[q][:, j, :], in0=th[j][:], scalar=0.5, in1=x1_half[q][:, j, :],
                                         op0=ALU.mult, op1=ALU.add).then_inc(v_res, 1)

            def step(i, q):
                if has(i + 1):
                    ah_low(i + 1, 1 - q)
                if has(i):
                    leaky(i, 1)
                if has(i - 1):
                    add_feats(i - 1, 1 - q, 1)
                if has(i + 2):
                    norm0(i + 2, q)
                    mask_term(i + 2, q)
                if has(i - 1):
                    residual1(i - 1, 1 - q, 1)
                if has(i + 1):
                    residual0(i + 1, 1 - q)
                if has(i):
                    inverse(i, 0)
                if has(i + 1):
                    norm1(i + 1, 1 - q)
                if has(i + 2):
                    scale0(i + 2, q)
                if has(i + 1):
                    hT_low(i + 1, 1 - q)
                if has(i):
                    inverse(i, 1)
                if has(i + 2):
                    h0_low(i + 2, q)
                if has(i + 1):
                    score_operands(i + 1)
                if has(i):
                    add_feats(i, q, 0)
                if has(i + 1):
                    mask_max(i + 1, 1 - q, 0)
                    leaky(i + 1, 0)
                    mask_max(i + 1, 1 - q, 1)
                if has(i):
                    residual1(i, q, 0)

            setup()
            pipeline(dve, step)

        @block.scalar
        def _(act):
            def setup():
                act.wait_ge(s_const, CONST)
                n = 0
                for h in range(H):
                    for dt in range(DT):
                        act.wait_ge(pe_set, n + 1)
                        act.activation(m_hi[:, dt, h * D:(h + 1) * D], gbank[n % 2][:, 0:D], ACT.Copy)\
                           .then_inc(a_set, 1)
                        n += 1
                act.activation(w0_hi[:], w0_f[:], ACT.Copy).then_inc(a_set, 1)
                act.wait_ge(v_set, n + 4)
                act.activation(u_hi[:], u_f[:], ACT.Copy).then_inc(a_set, 1)

            def h0_high(p, q):
                act.wait_ge(v_z0, 2 * (p + 1))
                if has(p - 2):
                    act.wait_ge(pe_ah, p - 1)
                    act.wait_ge(v_h0lo, p - 1)
                    act.wait_ge(g_aTlo, p - 1)
                act.activation(h0_hi[q][:], z0[q][:], ACT.Relu).then_inc(a_h0hi, 1)

            def aT_high(p, q):
                act.wait_ge(s_loaded[q], 8 * (p - q) + 16)
                if has(p - 2):
                    act.wait_ge(pe_ah, p - 1)
                    act.wait_ge(g_aTlo, p - 1)
                act.activation(aT_hi[q][:], adjT_of(q), ACT.Copy).then_inc(a_aThi, 1)

            def ah_high(p, q):
                act.wait_ge(pe_ah, p + 1)
                if has(p - 2):
                    act.wait_ge(pe_out0, p - 1)
                act.activation(ah_hi[q][:], front_jt[:], ACT.Copy).then_inc(a_ahhi, 1)

            def hT_high(p, q):
                act.wait_ge(pe_zT, p + 1)
                if has(p - 2):
                    act.wait_ge(pe_g, 2 * GC * (p - 1))
                act.activation(hT_hi[q][:], front_jt[:], ACT.Relu).then_inc(a_hThi, 1)

            def feats(p, q):
                act.wait_ge(v_z1, 2 * (p + 1))
                if has(p - 2):
                    act.wait_ge(v_y, 2 * (p - 1))
                act.activation(feats_c[q][:], z1[q][:], ACT.Relu).then_inc(a_relu, 1)

            def stationary(p):
                act.wait_ge(v_kqt, p + 1)
                if has(p - 1):
                    act.wait_ge(pe_s, 2 * p)
                for j in range(J):
                    act.activation(lq[j][:], kq_t[:].bitcast(F32), ACT.Identity, scale=coef[:, 5 + j:6 + j],
                                   bias=coef[:, 7 + j:8 + j]).then_inc(a_lq, 1)

            def keep_g(p, n):
                act.wait_ge(pe_g, 2 * GC * p + n + 1)
                if n % GC == 0 and has(p - 1):
                    act.wait_ge(pe_y, 2 * (p - 1) + n // GC + 1)
                act.activation(gf[n // GC][:, (n % GC) * BANK:(n % GC + 1) * BANK], gbank[n % 2][:], ACT.Copy)\
                   .then_inc(a_g, 1)

            def exp(p, j, h0, nh):
                if h0 == 0:
                    act.wait_ge(v_leaky, 2 * p + j + 1)
                    act.wait_ge(v_nlm, 2 * p + j + 1)
                    if has(p - 1):
                        act.wait_ge(v_rinv, 2 * (p - 1) + j + 1)
                for h in range(h0, h0 + nh):
                    e = act.activation(att[j][:, h, :], att[j][:, h, :], ACT.Exp, bias=nlm[j][:, h:h + 1],
                                       accum_out=esum[j][:, h:h + 1])
                if h0 + nh == H:
                    e.then_inc(a_exp, 1)

            def keep_pT(p, j):
                act.wait_ge(pe_pT, 2 * p + j + 1)
                if has(p - 1):
                    act.wait_ge(pe_y, 2 * (p - 1) + j + 1)
                for c in range(H // HC):
                    act.activation(pT[j][:, c * HC:(c + 1) * HC, :], sbank[j][:, c * BANK:(c + 1) * BANK]
                                   .rearrange("p (h n) -> p h n", h=HC), ACT.Copy).then_inc(a_pT, 1)

            def tanh(p, j):
                act.wait_ge(v_y, 2 * p + j + 1)
                if has(p - 1):
                    act.wait_ge(v_res, 2 * (p - 1) + j + 1)
                act.activation(th[j][:], y[j][:], ACT.Tanh, scale=0.5).then_inc(a_th, 1)

            def step(i, q):
                if has(i):
                    exp(i, 0, 0, 4)
                if has(i + 1):
                    ah_high(i + 1, 1 - q)
                if has(i):
                    keep_g(i, 0)
                    exp(i, 0, 4, 1)
                if has(i - 1):
                    tanh(i - 1, 1)
                if has(i):
                    keep_g(i, 1)
                    exp(i, 0, 5, 1)
                if has(i + 2):
                    aT_high(i + 2, q)
                if has(i):
                    keep_g(i, 2)
                    exp(i, 0, 6, 1)
                    keep_g(i, 3)
                    exp(i, 0, 7, 1)
                    exp(i, 1, 0, 1)
                    keep_g(i, 4)
                    exp(i, 1, 1, 2)
                    keep_g(i, 5)
                if has(i + 1):
                    hT_high(i + 1, 1 - q)
                if has(i):
                    keep_g(i, 6)
                    keep_pT(i, 0)
                    exp(i, 1, 3, 5)
                if has(i + 2):
                    h0_high(i + 2, q)
                if has(i + 1):
                    feats(i + 1, 1 - q)
                    stationary(i + 1)
                if has(i):
                    keep_pT(i, 1)
                    keep_g(i, 7)
                    tanh(i, 0)

            setup()
            pipeline(act, step)

        @block.gpsimd
        def _(gp):
            def setup():
                gp.memset(neg_half[:], -0.5)
                gp.memset(half[:], 0.5)
                gp.memset(eps[:], EPS)
                gp.memset(u_f[:], 0.0).then_inc(g_set, 1)
                for k in range(2):
                    gp.memset(fcb_rows[k][:], 0.0).then_inc(g_set, 1)
                gp.wait_ge(g_set, 3)
                gp.wait_ge(s_const, CONST)
                for k in range(2):
                    w = fcb_wide[k][:]
                    e = gp.tensor_copy(w, fcb[:, H * k:H * (k + 1)].unsqueeze(2).broadcast_to([P, H, P]))
                for t in range(H * DT):
                    h = t // DT
                    rows = fcb_rows[t // H][:, t % H, h:J * KQ:H]
                    e = gp.tensor_copy(rows, fcb[:, t:t + 1].broadcast_to([P, J * KQ // H]))
                e.then_inc(g_set, 1)

            def rstd(p, mv, ve, rs, ready, g_ve, g_rs):
                gp.wait_ge(ready, 2 * (p + 1))
                gp.tensor_tensor(ve[:], mv[:, :, 1], eps[:].broadcast_to([P, J]), ALU.add).then_inc(g_ve, 1)
                gp.wait_ge(g_ve, p + 1)
                gp.tensor_tensor(rs[:], ve[:], neg_half[:].broadcast_to([P, J]), ALU.pow).then_inc(g_rs, 1)

            def rstd0(p, q):
                rstd(p, mv0[q], ve0[q], rs0[q], v_mv0, g_ve0, g_rs0)

            def inputs(p, q):
                gp.wait_ge(s_loaded[q], 8 * (p - q) + 16)
                if has(p - 2):
                    gp.wait_ge(v_x1, p - 1)
                gp.tensor_tensor(xb[q][:], x_of(q), b0_row[:].unsqueeze(1).broadcast_to([P, J, D]), ALU.add)\
                  .then_inc(g_xb, 1)

            def aT_low(p, q):
                gp.wait_ge(a_aThi, p + 1)
                if has(p - 2):
                    gp.wait_ge(pe_ah, p - 1)
                gp.tensor_tensor(aT_lo[q][:], adjT_of(q), aT_hi[q][:].bitcast(F32), ALU.subtract).then_inc(g_aTlo, 1)

            def normalise(p, j):
                gp.wait_ge(v_rinv, 2 * p + j + 1)
                gp.tensor_tensor(att[j][:], att[j][:], rinv[j][:].unsqueeze(2).broadcast_to([P, H, P]), ALU.mult)\
                  .then_inc(g_norm, 1)

            def feats(p, q):
                gp.wait_ge(v_x1, p + 1)
                if has(p - 2):
                    gp.wait_ge(v_res, 2 * (p - 1))
                gp.tensor_tensor(x1_half[q][:], x1[q][:], half[:].unsqueeze(2).broadcast_to([P, J, D]), ALU.add)\
                  .then_inc(g_half, 1)
                gp.wait_ge(a_relu, p + 1)
                gp.tensor_tensor(feats_c[q][:], feats_c[q][:], c_row[:].unsqueeze(1).broadcast_to([P, J, D]), ALU.add)\
                  .then_inc(g_feats, 1)

            def step(i, q):
                if has(i + 2):
                    inputs(i + 2, q)
                    rstd0(i + 2, q)
                if has(i + 1):
                    rstd(i + 1, mv1[1 - q], ve1[1 - q], rs1[1 - q], v_mv1, g_ve1, g_rs1)
                if has(i):
                    normalise(i, 0)
                if has(i + 2):
                    aT_low(i + 2, q)
                if has(i):
                    normalise(i, 1)
                if has(i + 1):
                    feats(i + 1, 1 - q)

            setup()
            gp.wait_ge(v_set, SETUP_V)
            pipeline(gp, step)


def kernel(x, adj, L0_gnn_weight, L0_gnn_bias, L1_gnn_fc_w, L1_gnn_fc_b, L1_gnn_q_w, L1_gnn_q_b,
           L1_gnn_k_w, L1_gnn_k_b, L1_gnn_fp_w, L1_gnn_fp_b):
    import numpy as np
    import concourse.bacc as bacc
    from concourse.bass_utils import run_bass_kernel_spmd

    B = x.shape[0]
    NP = B // J
    x, adj = np.asarray(x), np.asarray(adj)

    def by_pair(a):
        return a.reshape(NP, J, P, -1).transpose(0, 2, 1, 3).reshape(NP, P, -1)

    def by_tile(a):
        a = np.asarray(a)
        return np.ascontiguousarray(a.reshape(-1, P, a.shape[-1]).transpose(1, 0, 2))

    graph = np.ascontiguousarray(np.concatenate(
        [by_pair(x), by_pair(adj), by_pair(adj.transpose(0, 2, 1))], axis=2))

    row = np.arange(P)
    j, kind, part = row // KQ, row % KQ // (2 * H), row % (2 * H) // H
    used = j < J
    head_mask = ((row[:, None] % H == np.arange(H)[None, :]) & used[:, None])
    head_mask = np.ascontiguousarray(np.repeat(head_mask[:, :, None], P, axis=2).astype(np.float32))
    key, query = used & (kind == 0), used & (kind == 1)
    coef = np.stack([key, query, -1.0 * (used & (part == 1)), key, query,
                     query & (j == 0), query & (j == 1), key & (j == 0), key & (j == 1), 0 * row],
                    axis=1).astype(np.float32)

    arrays = {
        "graph": graph,
        "identity": np.eye(P, dtype=np.float32),
        "head_mask": head_mask,
        "row_coef": coef,
        "w0": by_tile(L0_gnn_weight),
        "bias0": np.asarray(L0_gnn_bias),
        "fc_wT": by_tile(np.asarray(L1_gnn_fc_w).T),
        "fc_b": np.ascontiguousarray(np.asarray(L1_gnn_fc_b).reshape(-1, P).T),
        "qk_w": by_tile(np.concatenate([np.asarray(L1_gnn_k_w), np.asarray(L1_gnn_q_w)], axis=1)),
        "q_b": np.asarray(L1_gnn_q_b),
        "k_b": np.asarray(L1_gnn_k_b),
        "fp_w": by_tile(L1_gnn_fp_w),
        "fp_b": np.asarray(L1_gnn_fp_b),
    }
    nc = bacc.Bacc("TRN2", target_bir_lowering=False, num_devices=1)
    args = [nc.dram_tensor(f"{name}_dram", a.shape, F32, kind="ExternalInput").ap() for name, a in arrays.items()]
    out = nc.dram_tensor("out_dram", (NP, P, J * D), F32, kind="ExternalOutput").ap()
    gnn_pair(nc, *args, out)
    got = run_bass_kernel_spmd(nc, [{f"{n}_dram": a for n, a in arrays.items()}], core_ids=[0]).results[0]["out_dram"]
    return np.ascontiguousarray(got.reshape(NP, P, J, D).transpose(0, 2, 1, 3).reshape(B, P, D))
```
